# Optimizing a Trainium2 kernel written in Bass

```python
import numpy as np
import jax
import jax.numpy as jnp

def _softmax(x, axis=-1):
    return jax.nn.softmax(x, axis=axis)

def _gelu(x):
    return jax.nn.gelu(x, approximate=True)

def _silu(x):
    return jax.nn.silu(x)

def _sigmoid(x):
    return jax.nn.sigmoid(x)

def _layernorm(x, axis=-1, eps=1e-05):
    m = jnp.mean(x, axis=axis, keepdims=True)
    v = jnp.var(x, axis=axis, keepdims=True)
    return (x - m) / jnp.sqrt(v + eps)

def _scatter_add(tgt, idx, src, axis=0):
    return tgt.at[idx].add(src)

def _segment_sum(src, seg, n):
    return jax.ops.segment_sum(src, seg, n)
kernel_name = 'mk_xattn_ffn_d2_seqx_r8_5345d4'

def setup_inputs(seed: int=0):
    np.random.seed(seed)
    _w = jnp.asarray

    def _rec_inputs():
        import jax
        import jax.numpy as jnp
        _rk = jax.random.key(seed)
        x = -0.0003929 + 0.9999 * jax.random.normal(jax.random.fold_in(_rk, 1), (128, 64, 128), jnp.float32)
        _lenS = 64 - jax.random.randint(jax.random.fold_in(_rk, 7), (128,), 0, max(1, 64 // 4) + 1, jnp.int32)
        _lenS2 = 64 - jax.random.randint(jax.random.fold_in(_rk, 8), (128,), 0, max(1, 64 // 4) + 1, jnp.int32)
        _ctx_1024P = jax.random.normal(jax.random.fold_in(_rk, 11), (128, 16, 128), jnp.float32)
        _ctx_1024c = jax.random.dirichlet(jax.random.fold_in(_rk, 511), 0.3 * jnp.ones((16,), jnp.float32), (128, 64))
        _ctx_1024t = jnp.einsum('bsk,bkd->bsd', _ctx_1024c, _ctx_1024P)
        _ctx_1024t = _ctx_1024t * jax.lax.rsqrt(jnp.mean(jnp.square(_ctx_1024t)) + 1e-12) * 0.953939
        ctx_1024 = 2.81802e-05 + 1.00001 * (_ctx_1024t + 0.3 * jax.random.normal(jax.random.fold_in(_rk, 611), (128, 64, 128), jnp.float32))
        return (x, ctx_1024)
    x, ctx_1024 = _rec_inputs()

    def _L0_xattn_setup():
        import jax, jax.numpy as jnp
        import numpy as np
        import math
        D_MODEL = 128
        N_HEADS = 16
        C = 1
        B, L = (8, 256)

        def _glorot(key, fan):
            lim = np.sqrt(6.0 / (fan + fan)).astype(np.float32)
            return jax.random.uniform(key, (fan, fan), jnp.float32, -lim, lim)
        key = jax.random.key(seed)
        ks = jax.random.split(key, 7)
        queries = jax.random.normal(ks[0], (B, L, D_MODEL), jnp.float32)
        keys = jax.random.normal(ks[1], (B, L, D_MODEL), jnp.float32)
        values = jax.random.normal(ks[2], (B, L, D_MODEL), jnp.float32)
        wq = _glorot(ks[3], D_MODEL)
        wk = _glorot(ks[4], D_MODEL)
        wv = _glorot(ks[5], D_MODEL)
        wo = _glorot(ks[6], D_MODEL)
        return {'queries': queries, 'keys': keys, 'values': values, 'wq': wq, 'wk': wk, 'wv': wv, 'wo': wo}
    _L0_xattn_all = _L0_xattn_setup()
    _L0_xattn_in = {k: v for k, v in _L0_xattn_all.items() if k in ('wq', 'wk', 'wv', 'wo')}
    del _L0_xattn_all

    def _L0_ffn_setup():
        import jax, jax.numpy as jnp
        import numpy as np
        EPS = 1e-05

        def rmsnorm(x):
            return x * jax.lax.rsqrt(jnp.mean(x * x, axis=-1, keepdims=True) + EPS)

        def act_quant(x):
            scale = 127.0 / jnp.clip(jnp.max(jnp.abs(x), axis=-1, keepdims=True), 1e-05)
            q = jnp.clip(jnp.round(x * scale), -128.0, 127.0) / scale
            return x + jax.lax.stop_gradient(q - x)

        def weight_quant(w):
            scale = 1.0 / jnp.clip(jnp.mean(jnp.abs(w)), 1e-05)
            q = jnp.clip(jnp.round(w * scale), -1.0, 1.0) / scale
            return w + jax.lax.stop_gradient(q - w)

        def bitlinear(x, w, b):
            xq = act_quant(rmsnorm(x))
            wq = weight_quant(w)
            return jnp.einsum('bsd,fd->bsf', xq, wq) + b
        key = jax.random.key(seed)
        k0, k1, k2 = jax.random.split(key, 3)
        B, S, D, F = (2, 1024, 128, 512)
        x = jax.random.normal(k0, (B, S, D), dtype=jnp.float32)
        w1 = jax.random.normal(k1, (F, D), dtype=jnp.float32) * (1.0 / np.sqrt(D))
        b1 = jnp.zeros((F,), dtype=jnp.float32)
        w2 = jax.random.normal(k2, (D, F), dtype=jnp.float32) * (1.0 / np.sqrt(F))
        b2 = jnp.zeros((D,), dtype=jnp.float32)
        return {'x': x, 'w1': w1, 'b1': b1, 'w2': w2, 'b2': b2}
    _L0_ffn_all = _L0_ffn_setup()
    _L0_ffn_in = {k: v for k, v in _L0_ffn_all.items() if k in ('w1', 'b1', 'w2', 'b2')}
    del _L0_ffn_all

    def _L1_xattn_setup():
        import jax, jax.numpy as jnp
        import numpy as np
        DIM = 128
        DIM_HEAD = 64
        HEADS = 16
        INNER = DIM_HEAD * HEADS
        EPS = 1e-05

        def layer_norm(x, g, b):
            m = jnp.mean(x, axis=-1, keepdims=True)
            v = jnp.mean(jnp.square(x - m), axis=-1, keepdims=True)
            return (x - m) * jax.lax.rsqrt(v + EPS) * g + b
        key = jax.random.key(seed)
        ks = jax.random.split(key, 8)
        B, N_IMG, N_LAT = (4, 512, 64)
        std = 1.0 / np.sqrt(DIM)
        return {'image_embeds': jax.random.normal(ks[0], (B, N_IMG, DIM), dtype=jnp.float32), 'latents': jax.random.normal(ks[1], (B, N_LAT, DIM), dtype=jnp.float32), 'ln1_g': jnp.ones((DIM,), jnp.float32), 'ln1_b': jnp.zeros((DIM,), jnp.float32), 'ln2_g': jnp.ones((DIM,), jnp.float32), 'ln2_b': jnp.zeros((DIM,), jnp.float32), 'Wq': jax.random.normal(ks[2], (DIM, INNER), dtype=jnp.float32) * std, 'Wkv': jax.random.normal(ks[3], (DIM, 2 * INNER), dtype=jnp.float32) * std, 'Wo': jax.random.normal(ks[4], (INNER, DIM), dtype=jnp.float32) * std}
    _L1_xattn_all = _L1_xattn_setup()
    _L1_xattn_in = {k: v for k, v in _L1_xattn_all.items() if k in ('ln1_g', 'ln1_b', 'ln2_g', 'ln2_b', 'Wq', 'Wkv', 'Wo')}
    del _L1_xattn_all

    def _L1_ffn_setup():
        import jax, jax.numpy as jnp
        import numpy as np
        N_EMBED = 128
        FFN_HIDDEN = 512
        NUM_EXPERTS = 8
        TOP_K = 2
        key = jax.random.key(seed)
        ks = jax.random.split(key, 8)
        d, f, E = (N_EMBED, FFN_HIDDEN, NUM_EXPERTS)
        s_d = 1.0 / np.sqrt(d)
        s_f = 1.0 / np.sqrt(f)
        return {'x': jax.random.normal(ks[0], (2, 256, d), dtype=jnp.float32), 'Wg': jax.random.uniform(ks[1], (d, E), jnp.float32, -s_d, s_d), 'bg': jax.random.uniform(ks[2], (E,), jnp.float32, -s_d, s_d), 'W1': jax.random.uniform(ks[3], (E, d, f), jnp.float32, -s_d, s_d), 'b1': jax.random.uniform(ks[4], (E, f), jnp.float32, -s_d, s_d), 'W2': jax.random.uniform(ks[5], (E, f, d), jnp.float32, -s_f, s_f), 'b2': jax.random.uniform(ks[6], (E, d), jnp.float32, -s_f, s_f)}
    _L1_ffn_all = _L1_ffn_setup()
    _L1_ffn_in = {k: v for k, v in _L1_ffn_all.items() if k in ('Wg', 'bg', 'W1', 'b1', 'W2', 'b2')}
    del _L1_ffn_all
    return {'x': x, 'ctx_1024': ctx_1024, 'L0_xattn_wq': _L0_xattn_in['wq'], 'L0_xattn_wk': _L0_xattn_in['wk'], 'L0_xattn_wv': _L0_xattn_in['wv'], 'L0_xattn_wo': _L0_xattn_in['wo'], 'L0_ffn_w1': _L0_ffn_in['w1'], 'L0_ffn_b1': _L0_ffn_in['b1'], 'L0_ffn_w2': _L0_ffn_in['w2'], 'L0_ffn_b2': _L0_ffn_in['b2'], 'L1_xattn_ln1_g': _L1_xattn_in['ln1_g'], 'L1_xattn_ln1_b': _L1_xattn_in['ln1_b'], 'L1_xattn_ln2_g': _L1_xattn_in['ln2_g'], 'L1_xattn_ln2_b': _L1_xattn_in['ln2_b'], 'L1_xattn_Wq': _L1_xattn_in['Wq'], 'L1_xattn_Wkv': _L1_xattn_in['Wkv'], 'L1_xattn_Wo': _L1_xattn_in['Wo'], 'L1_ffn_Wg': _L1_ffn_in['Wg'], 'L1_ffn_bg': _L1_ffn_in['bg'], 'L1_ffn_W1': _L1_ffn_in['W1'], 'L1_ffn_b1': _L1_ffn_in['b1'], 'L1_ffn_W2': _L1_ffn_in['W2'], 'L1_ffn_b2': _L1_ffn_in['b2']}

def reference(x, ctx_1024, L0_xattn_wq, L0_xattn_wk, L0_xattn_wv, L0_xattn_wo, L0_ffn_w1, L0_ffn_b1, L0_ffn_w2, L0_ffn_b2, L1_xattn_ln1_g, L1_xattn_ln1_b, L1_xattn_ln2_g, L1_xattn_ln2_b, L1_xattn_Wq, L1_xattn_Wkv, L1_xattn_Wo, L1_ffn_Wg, L1_ffn_bg, L1_ffn_W1, L1_ffn_b1, L1_ffn_W2, L1_ffn_b2):
    import jax
    import jax.numpy as jnp

    def _L0_xattn_ref(queries, keys, values, wq, wk, wv, wo):
        import jax, jax.numpy as jnp
        import numpy as np
        import math
        D_MODEL = 128
        N_HEADS = 16
        C = 1
        B, L = (8, 256)

        def _glorot(key, fan):
            lim = np.sqrt(6.0 / (fan + fan)).astype(np.float32)
            return jax.random.uniform(key, (fan, fan), jnp.float32, -lim, lim)
        Bv, Lv, _ = queries.shape
        H = N_HEADS
        Dh = D_MODEL // N_HEADS
        Q = (queries @ wq).reshape(Bv, Lv, H, Dh).transpose(0, 2, 3, 1)
        K = (keys @ wk).reshape(Bv, Lv, H, Dh).transpose(0, 2, 3, 1)
        V = (values @ wv).reshape(Bv, Lv, H, Dh).transpose(0, 2, 3, 1)
        corr = jnp.fft.irfft(jnp.fft.rfft(Q, axis=-1) * jnp.conj(jnp.fft.rfft(K, axis=-1)), n=Lv, axis=-1)
        k_top = int(math.floor(C * math.log(Lv)))
        top_vals, top_idx = jax.lax.top_k(corr, k_top)
        w = jax.nn.softmax(top_vals, axis=-1)
        t = jnp.arange(Dh)
        out = jnp.zeros_like(V)
        for i in range(k_top):
            gather_idx = (t[None, None, :] - top_idx[..., i]) % Dh
            rolled = jnp.take_along_axis(V, gather_idx[..., None], axis=2)
            out = out + w[..., i, None] * rolled
        out = out.transpose(0, 2, 1, 3).reshape(Bv, Lv, D_MODEL)
        return out @ wo

    def _L0_ffn_ref(x, w1, b1, w2, b2):
        import jax, jax.numpy as jnp
        import numpy as np
        EPS = 1e-05

        def rmsnorm(x):
            return x * jax.lax.rsqrt(jnp.mean(x * x, axis=-1, keepdims=True) + EPS)

        def act_quant(x):
            scale = 127.0 / jnp.clip(jnp.max(jnp.abs(x), axis=-1, keepdims=True), 1e-05)
            q = jnp.clip(jnp.round(x * scale), -128.0, 127.0) / scale
            return x + jax.lax.stop_gradient(q - x)

        def weight_quant(w):
            scale = 1.0 / jnp.clip(jnp.mean(jnp.abs(w)), 1e-05)
            q = jnp.clip(jnp.round(w * scale), -1.0, 1.0) / scale
            return w + jax.lax.stop_gradient(q - w)

        def bitlinear(x, w, b):
            xq = act_quant(rmsnorm(x))
            wq = weight_quant(w)
            return jnp.einsum('bsd,fd->bsf', xq, wq) + b
        h = bitlinear(x, w1, b1)
        h = jax.nn.gelu(h, approximate=False)
        return bitlinear(h, w2, b2)

    def _L1_xattn_ref(image_embeds, latents, ln1_g, ln1_b, ln2_g, ln2_b, Wq, Wkv, Wo):
        import jax, jax.numpy as jnp
        import numpy as np
        DIM = 128
        DIM_HEAD = 64
        HEADS = 16
        INNER = DIM_HEAD * HEADS
        EPS = 1e-05

        def layer_norm(x, g, b):
            m = jnp.mean(x, axis=-1, keepdims=True)
            v = jnp.mean(jnp.square(x - m), axis=-1, keepdims=True)
            return (x - m) * jax.lax.rsqrt(v + EPS) * g + b
        B, S_lat, _ = latents.shape
        x = layer_norm(image_embeds, ln1_g, ln1_b)
        l = layer_norm(latents, ln2_g, ln2_b)
        q = l @ Wq
        kv_in = jnp.concatenate([x, l], axis=1)
        kv = kv_in @ Wkv
        k, v = jnp.split(kv, 2, axis=-1)

        def to_heads(t):
            return t.reshape(t.shape[0], t.shape[1], HEADS, DIM_HEAD).transpose(0, 2, 1, 3)
        q, k, v = (to_heads(q), to_heads(k), to_heads(v))
        scale = 1.0 / np.sqrt(np.sqrt(DIM_HEAD))
        w = jnp.einsum('bhqd,bhkd->bhqk', q * scale, k * scale)
        w = jax.nn.softmax(w.astype(jnp.float32), axis=-1).astype(q.dtype)
        out = jnp.einsum('bhqk,bhkd->bhqd', w, v)
        out = out.transpose(0, 2, 1, 3).reshape(B, S_lat, INNER)
        return out @ Wo

    def _L1_ffn_ref(x, Wg, bg, W1, b1, W2, b2):
        import jax, jax.numpy as jnp
        import numpy as np
        N_EMBED = 128
        FFN_HIDDEN = 512
        NUM_EXPERTS = 8
        TOP_K = 2
        gate_scores = jax.nn.softmax(x @ Wg + bg, axis=-1)
        topk_scores, topk_idx = jax.lax.top_k(gate_scores, TOP_K)
        topk_scores = topk_scores / (jnp.sum(topk_scores, axis=-1, keepdims=True) + 1e-08)
        onehot = jax.nn.one_hot(topk_idx, NUM_EXPERTS, dtype=x.dtype)
        combine_w = jnp.einsum('bsk,bske->bse', topk_scores, onehot)
        output = jnp.zeros_like(x)
        for e in range(NUM_EXPERTS):
            h = jax.nn.gelu(x @ W1[e] + b1[e])
            y = h @ W2[e] + b2[e]
            output = output + y * combine_w[..., e:e + 1]
        return output
    x = x + _L0_xattn_ref(_layernorm(x, axis=-1), ctx_1024, ctx_1024, L0_xattn_wq, L0_xattn_wk, L0_xattn_wv, L0_xattn_wo)
    x = x + _L0_ffn_ref(_layernorm(x, axis=-1), L0_ffn_w1, L0_ffn_b1, L0_ffn_w2, L0_ffn_b2)
    x = x + _L1_xattn_ref(ctx_1024, _layernorm(x, axis=-1), L1_xattn_ln1_g, L1_xattn_ln1_b, L1_xattn_ln2_g, L1_xattn_ln2_b, L1_xattn_Wq, L1_xattn_Wkv, L1_xattn_Wo)
    x = x + _L1_ffn_ref(_layernorm(x, axis=-1), L1_ffn_Wg, L1_ffn_bg, L1_ffn_W1, L1_ffn_b1, L1_ffn_W2, L1_ffn_b2)
    return x

_drawn_inputs = setup_inputs


def setup_inputs(seed=0):
    import zlib

    import numpy as np

    out = dict(_drawn_inputs(seed))
    spreads = {'L0_ffn_b1': (0.0, 0.1),
     'L0_ffn_b2': (0.0, 0.1),
     'L1_xattn_ln1_g': (1.0, 0.2),
     'L1_xattn_ln1_b': (0.0, 0.1),
     'L1_xattn_ln2_g': (1.0, 0.2),
     'L1_xattn_ln2_b': (0.0, 0.1)}
    factors = {'L1_ffn_bg': 3.303, 'L1_ffn_b1': 7.459, 'L1_ffn_b2': 5.267}
    for name, (base, spread) in spreads.items():
        noise = np.random.default_rng([zlib.crc32(name.encode()), seed]).standard_normal(out[name].shape)
        drawn = base * np.exp(spread * noise) if base else spread * noise
        out[name] = jnp.asarray(drawn.astype(out[name].dtype))
    for name, factor in factors.items():
        out[name] = (out[name] * factor).astype(out[name].dtype)
    return out
```

```python
import numpy as np
import concourse.bass as bass
from concourse import mybir
from contextlib import ExitStack

F32 = mybir.dt.float32
BF16 = mybir.dt.bfloat16
F16 = mybir.dt.float16
I32 = mybir.dt.int32
U32 = mybir.dt.uint32
ALU = mybir.AluOpType
ACT = mybir.ActivationFunctionType
AX = mybir.AxisListType

P = 128
BATCH, SEQ, D = 128, 64, 128
TILES = BATCH * SEQ // P
GT = 4
GROUPS = TILES // GT
NSEQ = 2 * GT
FF = 512
KB = FF // P
HEADS1 = 16
EXPERTS = 8
TOP = 4
EPS = 1e-5
ROUND = 12582912.0

C_DQ, C_DK, C_INV, C_ID, C_HM, C_IE, C_I8, C_ROW, C_DC = 0, 256, 512, 576, 704, 832, 864, 872, 936
C_ALL = 937


def constants():
    t, s = np.arange(SEQ), np.arange(SEQ // 2)
    w = 2 * np.pi / SEQ
    re = np.cos(w * np.outer(t, s))
    im = -np.sin(w * np.outer(t, s))
    im[:, 0] = (-1.0) ** t
    fq = np.concatenate([re, im, im, re], 1)
    fk = np.concatenate([re, im, re, im], 1)
    c, n = 2 * np.cos(w * np.outer(s, t)), 2 * np.sin(w * np.outer(s, t))
    a, b = c.copy(), c.copy()
    a[0], b[0] = 1.0, (-1.0) ** t
    inv = np.concatenate([a, b, -n, n], 0) / SEQ
    out = np.zeros((P, C_ALL))
    for u in range(2):
        out[64 * u:64 * u + 64, C_DQ + 128 * u:C_DQ + 128 * u + 128] = fq
        out[64 * (1 - u):64 * (1 - u) + 64, C_DK + 128 * u:C_DK + 128 * u + 128] = fk
    out[:, C_INV:C_INV + 64] = inv
    out[:, C_ID:C_ID + P] = np.eye(P)
    ch = np.arange(P)
    by_parity = np.argsort(ch // 8 % 2, kind="stable")
    out[:, C_HM:C_HM + P] = ch[:, None] // 8 == by_parity[None, :] // 8
    out[ch, C_ROW + ch % 8 * 8 + ch // 16] = 1
    out[:, C_IE:C_IE + 32] = np.repeat(np.arange(8), TOP)[None]
    out[:, C_I8:C_I8 + 8] = np.arange(8)[None]
    out[:, C_DC] = ch % 8 + 64
    return out.astype(np.float32)


def rep(ap, axis, n):
    shape = list(ap.shape)
    return ap.unsqueeze(axis).broadcast_to(shape[:axis] + [n] + shape[axis:])


def known(*values):
    return all(isinstance(v, int) for v in values)


def walk(eng, first, last, unroll, lo, hi, step):
    for n in range(first, lo):
        step(n // unroll, n % unroll)
    with eng.Fori(lo // unroll, hi // unroll) as i:
        for k in range(unroll):
            step(i, k)
    for n in range(hi, last):
        step(n // unroll, n % unroll)


def wait(eng, sem, value):
    if not known(value) or value > 0:
        eng.wait_ge(sem, value)


def parts_product(pe, out, lhs, rhs, start=True, stop=True):
    pe.matmul(out, lhs[0], rhs[0], start=start, stop=False)
    pe.matmul(out, lhs[0], rhs[1], start=False, stop=False)
    return pe.matmul(out, lhs[1], rhs[0], start=False, stop=stop)


class Shared:
    pass



def load_weights(nc, s, dram):
    sem = s.sem
    w_const, w_l0, w_bit, w_attn, w_moe = [sem(n) for n in ("w_const", "w_l0", "w_bit", "w_attn", "w_moe")]
    s.w_moe = w_moe
    bit_abs, bit_sum, bit_q, bit_t, bit_tc = [sem(n) for n in ("bit_abs", "bit_sum", "bit_q", "bit_t", "bit_tc")]
    pr_t, pr_tc, pr_m, pr_mc = [sem(n) for n in ("prep_transposed", "prep_copied", "prep_fused", "prep_stored")]
    b1_t = sem("moe_b1_transposed")
    with ExitStack() as ctx:
        sb = lambda name, shape, dt=F32: ctx.enter_context(nc.sbuf_tensor(name, shape, dt))
        w1 = sb("w1_raw", [P, KB, D])
        w2 = sb("w2_raw", [P, FF])
        wt = sb("w_scaled", [P, 2, FF])
        wb = sb("w_ternary", [P, 2, FF], BF16)
        absum = sb("w_abs_sum", [P, 2])
        inv = sb("w_inv_scale", [P, 2])
        wq = sb("Wq_raw", [P, 1024])
        wkv = sb("Wkv_raw", [P, 2048])
        wo = sb("Wo_raw", [P, 8, D])
        wT = sb("W_transposed", [P, 3, 8, P])
        b1row = sb("moe_b1_rows", [32, P])
        ones = sb("ones", [P, P])
        block = ctx.enter_context(nc.Block())

        @block.sync
        def _(sp):
            sp.dma_start(s.const[:], dram["const"]).then_inc(w_const, 16)
            sp.dma_start(w1[:], dram["L0_ffn_w1"].rearrange("(k p) d -> p k d", p=P)).then_inc(w_bit, 16)
            sp.dma_start(w2[:], dram["L0_ffn_w2"]).then_inc(w_bit, 16)
            sp.dma_start(wq[:], dram["L1_xattn_Wq"]).then_inc(w_attn, 16)
            sp.dma_start(wkv[:], dram["L1_xattn_Wkv"]).then_inc(w_attn, 16)
            sp.dma_start(wo[:], dram["L1_xattn_Wo"].rearrange("(k p) d -> p k d", p=P)).then_inc(w_attn, 16)
            sp.dma_start(b1row[:], dram["L1_ffn_b1"].rearrange("e (k p) -> (e k) p", p=P)).then_inc(w_attn, 16)
            for n, name in enumerate(("wq", "wk", "wv", "wo")):
                src = dram["L0_xattn_" + name].rearrange("i (a b e) -> i a b e", b=2, e=8)
                to = s.w_l0[:, n, :]
                if name == "wv":
                    for par in range(2):
                        sp.dma_start(to[:, 64 * par:64 * par + 64].rearrange("i (a e) -> i a e", e=8), src[:, :, par, :]).then_inc(w_l0, 16)
                else:
                    sp.dma_start(to, dram["L0_xattn_" + name]).then_inc(w_l0, 16)
            for name, to in (("L0_ffn_b1", s.bit_b1), ("L0_ffn_b2", s.bit_b2), ("L1_ffn_bg", s.moe_bg)):
                sp.dma_start(to[:], dram[name].partition_broadcast(P)).then_inc(w_l0, 16)
            for u in range(2):
                for half in range(2):
                    of = "ln2" if half == u else "ln1"
                    rows = slice(64 * half, 64 * half + 64)
                    sp.dma_start(s.ln_g[rows, u, :], dram[f"L1_xattn_{of}_g"].partition_broadcast(64)).then_inc(w_l0, 16)
                    sp.dma_start(s.ln_b[rows, u, :], dram[f"L1_xattn_{of}_b"].partition_broadcast(64)).then_inc(w_l0, 16)
            sp.dma_start(s.moe_wg[:], dram["L1_ffn_Wg"]).then_inc(w_moe, 16)
            sp.dma_start(s.moe_b2[:], dram["L1_ffn_b2"]).then_inc(w_moe, 16)
            for e in range(EXPERTS):
                sp.dma_start(s.moe_w1[:, e, :], dram["L1_ffn_W1"][e, :, :]).then_inc(w_moe, 16)
                sp.dma_start(s.moe_w2[:, e, :, :], dram["L1_ffn_W2"][e, :, :].rearrange("(k p) d -> p k d", p=P)).then_inc(w_moe, 16)
            sp.wait_ge(w_l0, 16 * 16)

        @block.gpsimd
        def _(pool):
            pool.memset(s.mhalf[:], -0.5)
            pool.memset(s.eps[:], EPS)
            pool.memset(s.eps_ff[:], EPS * FF)
            pool.memset(ones[:], 1.0).then_inc(bit_abs, 1)

        @block.vector
        def _(dve):
            dve.wait_ge(w_const, 16)
            dve.tensor_copy(s.ident_b[:], s.ident)
            dve.wait_ge(w_bit, 32)
            dve.tensor_reduce(absum[:, 0:1], w1[:].rearrange("p k d -> p (k d)"), AX.X, ALU.add, apply_absolute_value=True)
            dve.tensor_reduce(absum[:, 1:2], w2[:], AX.X, ALU.add, apply_absolute_value=True).then_inc(bit_abs, 1)
            dve.wait_ge(bit_sum, 1)
            dve.tensor_scalar(s.bit_ws[:], s.pb[0][:, 0:2], 1.0 / (FF * D), EPS, ALU.mult, ALU.max)
            dve.drain()
            dve.reciprocal(inv[:], s.bit_ws[:])
            dve.drain()
            dve.tensor_scalar(wt[:, 0, :], w1[:].rearrange("p k d -> p (k d)"), inv[:, 0:1], ROUND, ALU.mult, ALU.add)
            dve.tensor_scalar(wt[:, 1, :], w2[:], inv[:, 1:2], ROUND, ALU.mult, ALU.add)
            dve.drain()
            dve.tensor_scalar(wt[:], wt[:], ROUND, -1.0, ALU.subtract, ALU.max)
            dve.drain()
            dve.tensor_scalar(wb[:], wt[:], 1.0, None, ALU.min).then_inc(bit_q, 1)
            dve.wait_ge(bit_t, 1)
            t1 = s.pb[1][:].bitcast(BF16)
            dve.tensor_copy(s.bit_w1[:], t1[:, 0:FF])
            dve.tensor_copy(s.bit_w2[:].rearrange("p k d -> p (k d)"), t1[:, FF:2 * FF]).then_inc(bit_tc, 1)
            dve.wait_ge(b1_t, 1)
            dve.tensor_copy(s.moe_b1[:], s.pb[1][:, 0:32])
            for n in range(6):
                dve.wait_ge(pr_t, n + 1)
                dve.tensor_copy(wT[:, n // 2, 4 * (n % 2):4 * (n % 2) + 4, :], s.pb[2 + n % 2][:].rearrange("p (k c) -> p k c", k=4)).then_inc(pr_tc, 1)
            for n in range(8):
                dve.wait_ge(pr_m, n + 1)
                src = s.pb[4 + n % 2][:].rearrange("p (k c) -> p k c", k=4)
                heads = slice(8 * (n % 4 // 2) + n % 2, 8 * (n % 4 // 2) + n % 2 + 7, 2)
                if n < 4:
                    dve.tensor_scalar(s.qk[:, heads, :], src, 0.125, None, ALU.mult).then_inc(pr_mc, 1)
                else:
                    dve.tensor_copy(s.vo[:, heads, :], src).then_inc(pr_mc, 1)

        @block.tensor
        def _(pe):
            pe.wait_ge(bit_abs, 2)
            pe.matmul(s.pb[0][:, 0:2], ones[:], absum[:], start=True, stop=True).then_inc(bit_sum, 1)
            pe.wait_ge(bit_q, 1)
            t1 = s.pb[1][:].bitcast(BF16)
            for n in range(2):
                for k in range(KB):
                    at = FF * n + P * k
                    last = pe.transpose(t1[:, at:at + P], wb[:, n, P * k:P * k + P], s.ident_b[:])
            last.then_inc(bit_t, 1)
            pe.wait_ge(w_attn, 64)
            pe.wait_ge(bit_tc, 1)
            pe.transpose(s.pb[1][:, 0:32], b1row[:], s.ident[0:32, 0:32]).then_inc(b1_t, 1)
            for n in range(6):
                src = wq[:] if n < 2 else wkv[:]
                at = 512 * (n if n < 2 else n - 2)
                if n >= 2:
                    pe.wait_ge(pr_tc, n - 1)
                for k in range(4):
                    last = pe.transpose(s.pb[2 + n % 2][:, P * k:P * k + P], src[:, at + P * k:at + P * k + P], s.ident)
                last.then_inc(pr_t, 1)
            pe.wait_ge(pr_tc, 6)
            for n in range(8):
                if n >= 2:
                    pe.wait_ge(pr_mc, n - 1)
                for k in range(4):
                    h = 8 * (n % 4 // 2) + 2 * k + n % 2
                    rows = slice(64 * (h % 2), 64 * (h % 2) + 64)
                    a, b = (wT[rows, 0, h // 2, :], wT[rows, 1, h // 2, :]) if n < 4 else (wT[rows, 2, h // 2, :], wo[rows, h // 2, :])
                    last = pe.matmul(s.pb[4 + n % 2][:, P * k:P * k + P], a, b, start=True, stop=True)
                last.then_inc(pr_m, 1)



def autocorrelation(nc, s, x_in, ctx_in):
    sem = s.sem
    x_loaded = [sem(f"a_x_loaded{n}") for n in range(2)]
    c_loaded = [sem(f"a_c_loaded{n}") for n in range(2)]
    names = ("stats rstd xn spec spec_copied qk kk_copied prod corr top ev exp weights mix ct ct_copied vt vt_copied "
             "rows rows_copied mixed mixed_copied out x1")
    m = {n: sem("a_" + n) for n in names.split()}
    with ExitStack() as ctx:
        sb = lambda name, shape, dt=F32: ctx.enter_context(nc.sbuf_tensor(name, shape, dt))
        cs = [sb(f"a_ctx{n}", [P, GT, D]) for n in range(2)]
        xn = [sb(f"a_xn{n}", [P, GT, D]) for n in range(2)]
        spec = [sb(f"a_spec{n}", [P, GT, 4, P]) for n in range(2)]
        kk = [sb(f"a_kk{n}", [P, 4, P]) for n in range(2)]
        prod = [sb(f"a_prod{n}", [P, NSEQ, P]) for n in range(2)]
        mix = [sb(f"a_mix{n}", [P, NSEQ, P]) for n in range(2)]
        ct = sb("a_ctxT", [P, GT * P])
        vt = sb("a_vT", [P, GT * P])
        rows_sb = sb("a_rows", [P, NSEQ, SEQ])
        mixed = sb("a_mixed", [P, NSEQ, SEQ])
        bst = sb("a_bn", [P, GT, 6])
        mv = sb("a_mv", [P, GT, 2])
        rstd = sb("a_rstd", [P, GT])
        corr = sb("a_corr", [P, NSEQ, SEQ])
        v8 = sb("a_top8", [P, NSEQ, 8])
        ix = sb("a_idx8", [P, NSEQ, 8], U32)
        ev = sb("a_ev", [P, NSEQ, TOP])
        ew = sb("a_ew", [P, NSEQ, TOP])
        wsum = sb("a_wsum", [P, NSEQ])
        roll = sb("a_roll", [P, NSEQ, TOP], I32)
        hit = sb("a_hit", [P, NSEQ * 8, TOP])
        wts = sb("a_weights", [P, NSEQ, 8])
        block = ctx.enter_context(nc.Block())
        SP_B = s.pb[0:2]
        QQ, KK, CORR, MIX, CV, OUT = s.pb[2:8]
        cv = ctx_in.rearrange("(t two) s d -> two s t d", two=2)
        xv = x_in.rearrange("(t two) s d -> (two s) t d", two=2)

        @block.sync
        def _(sp):
            def step(i, k):
                g = 2 * i + k
                if not (known(i) and i == 0):
                    sp.wait_ge(x_loaded[k], 16 * i)
                    sp.wait_ge(m["ct"], g - 1)
                sp.dma_start(s.xg(g), xv[:, bass.ts(g, GT), :]).then_inc(x_loaded[k], 16)
                sp.dma_start(cs[k][0:64, :, :], cv[1, :, bass.ts(g, GT), :]).then_inc(c_loaded[k], 16)
                sp.dma_start(cs[k][64:128, :, :], cv[0, :, bass.ts(g, GT), :]).then_inc(c_loaded[k], 16)
            walk(sp, 0, GROUPS, 2, 2, GROUPS, step)

        @block.gpsimd
        def _(pool):
            def norm(g):
                wait(pool, m["stats"], g + 1)
                pool.tensor_tensor(rstd[:], mv[:, :, 1], s.eps[:, 0:GT], ALU.add)
                pool.drain()
                pool.tensor_tensor(rstd[:], rstd[:], s.mhalf[:, 0:GT], ALU.pow).then_inc(m["rstd"], 1)

            def step(i, k):
                g = 2 * i + k
                if not (known(i) and g + 1 >= GROUPS):
                    norm(g + 1)
                pool.wait_ge(m["weights"], g + 1)
                wait(pool, m["rows"], g - 1)
                pool.tensor_tensor(mix[k][:].rearrange("p b (h e) -> p b h e", e=8), rep(wts[:], 2, 16),
                                   rep(s.headmask.rearrange("p (h e) -> p h e", e=8), 1, NSEQ), ALU.mult).then_inc(m["mix"], 1)
            norm(0)
            walk(pool, 0, GROUPS, 2, 2, GROUPS - 2, step)

        @block.vector
        def _(dve):
            def prepare(i, k):
                g = 2 * i + k
                dve.wait_ge(x_loaded[k], 16 * (i + 1))
                for j in range(GT):
                    dve.bn_stats(bst[:, j, :], s.xg(g)[:, j, :])
                dve.drain()
                for j in range(GT):
                    last = dve.bn_aggr(mv[:, j, :], bst[:, j, :])
                last.then_inc(m["stats"], 1)
                dve.wait_ge(m["rstd"], g + 1)
                wait(dve, m["spec"], 4 * (g - 1))
                for j in range(GT):
                    last = dve.tensor_scalar(xn[k][:, j, :], s.xg(g)[:, j, :], mv[:, j, 0:1], rstd[:, j:j + 1], ALU.subtract, ALU.mult)
                last.then_inc(m["xn"], 1)

            def add_out(g):
                dve.drain()
                dve.wait_ge(m["out"], g + 1)
                dve.tensor_tensor(s.xg(g), s.xg(g), OUT[:].rearrange("p (j d) -> p j d", j=GT), ALU.add).then_inc(m["x1"], 1)

            def step(i, k):
                g = 2 * i + k
                if not (known(i) and g >= GROUPS):
                    for h in range(2):
                        dve.wait_ge(m["kk_copied"], 2 * g + h + 1)
                        if h == 0:
                            wait(dve, m["corr"], g - 1)
                        dve.tensor_tensor(prod[k][:, 4 * h:4 * h + 4, :], QQ[:].rearrange("p (b c) -> p b c", b=4), kk[h][:],
                                          ALU.mult).then_inc(m["prod"], 1)
                    if not (known(i) and g + 1 >= GROUPS):
                        prepare(i + (k + 1) // 2, (k + 1) % 2)
                    dve.wait_ge(m["corr"], g + 1)
                    dve.tensor_copy(corr[:].rearrange("p b l -> p (b l)"), CORR[:]).then_inc(m["top"], 1)
                    dve.drain()
                    for b in range(NSEQ):
                        dve.max(v8[:, b, :], corr[:, b, :])
                    dve.drain()
                    for b in range(NSEQ):
                        dve.max_index(ix[:, b, :], v8[:, b, :], corr[:, b, :])
                    dve.tensor_tensor(ev[:], v8[:, :, 0:TOP], v8[:, :, 0:1].broadcast_to([P, NSEQ, TOP]), ALU.subtract).then_inc(m["ev"], 1)
                    dve.drain()
                    dve.tensor_scalar(roll[:], ix[:, :, 0:TOP], -1.0, s.chan, ALU.mult, ALU.add)
                    dve.drain()
                    dve.tensor_scalar(roll[:], roll[:], 7, None, ALU.bitwise_and)
                    dve.drain()
                    dve.tensor_tensor(hit[:].rearrange("p (b e) i -> p b e i", b=NSEQ), rep(roll[:], 2, 8), rep(s.iota_e, 1, NSEQ), ALU.is_equal)
                    dve.wait_ge(m["exp"], g + 1)
                    dve.tensor_reduce(wsum[:], ew[:], AX.X, ALU.add)
                    dve.drain()
                    dve.reciprocal(wsum[:], wsum[:])
                    dve.drain()
                    dve.tensor_tensor(ev[:], ew[:], rep(wsum[:], 2, TOP), ALU.mult)
                    dve.drain()
                    dve.tensor_tensor(hit[:].rearrange("p (b e) i -> p b e i", b=NSEQ), hit[:].rearrange("p (b e) i -> p b e i", b=NSEQ),
                                      rep(ev[:], 2, 8), ALU.mult)
                    dve.drain()
                    wait(dve, m["mix"], g)
                    dve.tensor_reduce(wts[:].rearrange("p b e -> p (b e)"), hit[:], AX.X, ALU.add).then_inc(m["weights"], 1)
                if not (known(i) and g == 0):
                    add_out(g - 1)
            prepare(0, 0)
            walk(dve, 0, GROUPS + 1, 2, 2, GROUPS - 2, step)

        @block.scalar
        def _(act):
            def step(i, k):
                g = 2 * i + k
                new, old = not (known(i) and g >= GROUPS), not (known(i) and g == 0)
                if new:
                    wait(act, m["qk"], 2 * (g - 1))
                    for j in range(GT):
                        act.wait_ge(m["spec"], 4 * g + j + 1)
                        act.activation(spec[k][:, j, :, :], SP_B[j % 2][:].rearrange("p (a c) -> p a c", a=4), ACT.Copy).then_inc(m["spec_copied"], 1)
                if old:
                    act.wait_ge(m["ct"], g)
                    wait(act, m["vt"], g - 1)
                    act.activation(ct[:], CV[:], ACT.Copy).then_inc(m["ct_copied"], 1)
                for h in range(2):
                    if new:
                        act.wait_ge(m["qk"], 2 * g + h + 1)
                        wait(act, m["prod"], 2 * g + h - 1)
                        act.activation(kk[h][:], KK[:].rearrange("p (b c) -> p b c", b=4), ACT.Copy).then_inc(m["kk_copied"], 1)
                    if old and h == 0:
                        act.wait_ge(m["vt"], g)
                        wait(act, m["mixed"], g - 1)
                        act.activation(vt[:], CV[:], ACT.Copy).then_inc(m["vt_copied"], 1)
                        act.wait_ge(m["rows"], g)
                        act.activation(rows_sb[:].rearrange("p b r -> p (b r)"), MIX[:], ACT.Copy).then_inc(m["rows_copied"], 1)
                if old:
                    act.wait_ge(m["mixed"], g)
                    wait(act, m["out"], g - 1)
                    act.activation(mixed[:].rearrange("p b r -> p (b r)"), MIX[:], ACT.Copy).then_inc(m["mixed_copied"], 1)
                if new:
                    act.wait_ge(m["ev"], g + 1)
                    wait(act, m["weights"], g)
                    act.activation(ew[:], ev[:], ACT.Exp).then_inc(m["exp"], 1)
            walk(act, 0, GROUPS + 1, 2, 2, GROUPS - 2, step)

        @block.tensor
        def _(pe):
            wq, wk, wv, wo = (s.w_l0[:, n, :] for n in range(4))

            def step(i, k):
                g = 2 * i + k
                new, old = not (known(i) and g >= GROUPS), not (known(i) and g == 0)
                if new:
                    pe.wait_ge(m["xn"], g + 1)
                    pe.wait_ge(c_loaded[k], 32 * (i + 1))
                    for j in range(GT):
                        wait(pe, m["spec_copied"], 4 * g + j - 1)
                        pe.matmul(SP_B[j % 2][:, 0:256], xn[k][:, j, :], s.dft_q, start=True, stop=True)
                        pe.matmul(SP_B[j % 2][:, 256:512], cs[k][:, j, :], s.dft_k, start=True, stop=True).then_inc(m["spec"], 1)
                if old:
                    wait(pe, m["vt_copied"], g - 1)
                    for j in range(GT):
                        last = pe.transpose(CV[:, P * j:P * j + P], cs[1 - k][:, j, :], s.ident)
                    last.then_inc(m["ct"], 1)
                for h in range(2):
                    if new:
                        pe.wait_ge(m["spec_copied"], 4 * g + 2 * h + 2)
                        wait(pe, m["prod"], 2 * g + h)
                        for b in range(4):
                            pe.matmul(QQ[:, P * b:P * b + P], spec[k][:, 2 * h + b // 2, b % 2, :], wq, start=True, stop=True)
                        if old and h == 1:
                            pe.wait_ge(m["rows_copied"], g)
                            pe.wait_ge(m["vt_copied"], g)
                        for b in range(4):
                            last = pe.matmul(KK[:, P * b:P * b + P], spec[k][:, 2 * h + b // 2, 2 + b % 2, :], wk, start=True, stop=True)
                        last.then_inc(m["qk"], 1)
                    if old and h == 0:
                        pe.wait_ge(m["ct_copied"], g)
                        pe.matmul(CV[:], wv, ct[:], start=True, stop=True).then_inc(m["vt"], 1)
                        pe.wait_ge(m["mix"], g)
                        wait(pe, m["mixed_copied"], g - 1)
                        for b in range(NSEQ):
                            last = pe.matmul(MIX[:, SEQ * b:SEQ * b + SEQ], mix[1 - k][:, b, :], s.row_of, start=True, stop=True)
                        last.then_inc(m["rows"], 1)
                if old:
                    if not new:
                        pe.wait_ge(m["rows_copied"], g)
                        pe.wait_ge(m["vt_copied"], g)
                    for j in range(GT):
                        for u in range(2):
                            at, b = P * j + 64 * (1 - u), 2 * j + u
                            for par in range(2):
                                half = slice(64 * par, 64 * par + 64)
                                last = pe.matmul(MIX[half, SEQ * b:SEQ * b + SEQ], vt[half, at:at + 64], rows_sb[half, b, :], start=True, stop=True)
                    last.then_inc(m["mixed"], 1)
                if new:
                    pe.wait_ge(m["prod"], 2 * g + 2)
                    wait(pe, m["top"], g)
                    for b in range(NSEQ):
                        last = pe.matmul(CORR[:, 64 * b:64 * b + 64], prod[k][:, b, :], s.dft_inv, start=True, stop=True)
                    last.then_inc(m["corr"], 1)
                if old:
                    pe.wait_ge(m["mixed_copied"], g)
                    wait(pe, m["x1"], g - 1)
                    for j in range(GT):
                        last = pe.matmul(OUT[:, P * j:P * j + P], mixed[:, 2 * j:2 * j + 2, :], wo, start=True, stop=True)
                    last.then_inc(m["out"], 1)
            walk(pe, 0, GROUPS + 1, 2, 2, GROUPS - 2, step)



def bit_ffn(nc, s):
    sem = s.sem
    names = ("mv r1 amax scale q qt qt_copied h hb gelu sq amax2 scale2 q2 q2t q2t_copied product x2 xb2")
    m = {n: sem("b_" + n) for n in names.split()}
    with ExitStack() as ctx:
        sb = lambda name, shape, dt=F32: ctx.enter_context(nc.sbuf_tensor(name, shape, dt))
        bst = sb("b_bn", [P, GT, 6])
        mv = sb("b_mv", [P, GT, 2])
        tmp = sb("b_tmp", [P, GT])
        r1 = sb("b_r1", [P, GT])
        rr = sb("b_rr", [P, GT])
        am = sb("b_amax", [P, GT])
        mx = sb("b_mx", [P, GT])
        qs = sb("b_qs", [P, GT])
        deq = [sb(f"b_deq{n}", [P, GT]) for n in range(2)]
        xc = sb("b_xc", [P, GT, D])
        xr = sb("b_xr", [P, GT, D])
        qb = [sb(f"b_q{n}", [P, GT, D], BF16) for n in range(2)]
        qt = [sb(f"b_qt{n}", [P, GT * P], BF16) for n in range(2)]
        hb = [sb(f"b_hb{n}", [P, FF]) for n in range(2)]
        ge = [sb(f"b_gelu{n}", [P, GT, FF]) for n in range(2)]
        junk = sb("b_junk", [P, 2, FF])
        ssq = sb("b_ssq", [P, GT])
        am2 = sb("b_amax2", [P, GT])
        tmp2 = sb("b_tmp2", [P, GT])
        mx2 = sb("b_mx2", [P, GT])
        qs2 = sb("b_qs2", [P, GT])
        deq2 = [sb(f"b_deq2{n}", [P, GT]) for n in range(2)]
        q2 = [sb(f"b_q2{n}", [P, GT, FF], BF16) for n in range(2)]
        q2t = [sb(f"b_q2t{n}", [P, KB, P], BF16) for n in range(2)]
        block = ctx.enter_context(nc.Block())
        QT = s.pb[0][:].bitcast(BF16)
        HB = s.pb[1:3]
        T2 = [s.pb[3][:].bitcast(BF16), s.pb[4][:].bitcast(BF16)]
        OUT = s.pb[5]

        @block.gpsimd
        def _(pool):
            def first(g, k):
                pool.wait_ge(m["mv"], g + 1)
                pool.tensor_tensor(tmp[:], mv[:, :, 1], s.eps[:, 0:GT], ALU.add)
                pool.drain()
                pool.tensor_tensor(r1[:], tmp[:], s.mhalf[:, 0:GT], ALU.pow)
                pool.drain()
                pool.tensor_tensor(tmp[:], r1[:], r1[:], ALU.mult)
                pool.drain()
                pool.tensor_tensor(tmp[:], tmp[:], mv[:, :, 1], ALU.mult)
                pool.drain()
                pool.tensor_scalar(tmp[:], tmp[:], EPS, None, ALU.add)
                pool.drain()
                pool.tensor_tensor(tmp[:], tmp[:], s.mhalf[:, 0:GT], ALU.pow)
                pool.drain()
                pool.tensor_tensor(rr[:], tmp[:], r1[:], ALU.mult)
                pool.tensor_tensor(s.xg(g), s.xg(g), rep(s.bit_b2[:], 1, GT), ALU.add).then_inc(m["xb2"], 1)
                pool.drain()
                pool.wait_ge(m["amax"], g + 1)
                pool.tensor_tensor(mx[:], am[:], rr[:], ALU.mult)
                pool.drain()
                pool.tensor_scalar(mx[:], mx[:], 1e-5, None, ALU.max).then_inc(m["r1"], 1)
                pool.drain()
                pool.tensor_scalar(deq[k][:], mx[:], 1.0 / 127.0, None, ALU.mult)
                pool.drain()
                pool.tensor_scalar(deq[k][:], deq[k][:], s.bit_ws[:, 0:1], None, ALU.mult).then_inc(m["scale"], 1)

            def second(g, k):
                pool.wait_ge(m["sq"], 4 * g + 4)
                pool.tensor_tensor(tmp2[:], ssq[:], s.eps_ff[:, 0:GT], ALU.add)
                pool.drain()
                pool.tensor_scalar(tmp2[:], tmp2[:], 1.0 / FF, None, ALU.mult)
                pool.drain()
                pool.tensor_tensor(tmp2[:], tmp2[:], s.mhalf[:, 0:GT], ALU.pow)
                pool.drain()
                wait(pool, m["x2"], g - 1)
                pool.wait_ge(m["amax2"], 4 * g + 4)
                pool.tensor_tensor(mx2[:], am2[:], tmp2[:], ALU.mult)
                pool.drain()
                pool.tensor_scalar(mx2[:], mx2[:], 1e-5, None, ALU.max)
                pool.drain()
                pool.tensor_scalar(deq2[k][:], mx2[:], 1.0 / 127.0, None, ALU.mult)
                pool.drain()
                pool.tensor_scalar(deq2[k][:], deq2[k][:], s.bit_ws[:, 1:2], None, ALU.mult).then_inc(m["scale2"], 1)

            def step(i, k):
                g = 2 * i + k
                if not (known(i) and g + 1 >= GROUPS):
                    first(g + 1, (k + 1) % 2)
                second(g, k)
            first(0, 0)
            walk(pool, 0, GROUPS, 2, 2, GROUPS - 2, step)

        @block.vector
        def _(dve):
            def prepare(g):
                for j in range(GT):
                    dve.bn_stats(bst[:, j, :], s.xg(g)[:, j, :])
                dve.drain()
                for j in range(GT):
                    dve.bn_aggr(mv[:, j, :], bst[:, j, :])
                dve.drain()
                dve.tensor_tensor(xc[:], s.xg(g), mv[:, :, 0:1].broadcast_to([P, GT, D]), ALU.subtract).then_inc(m["mv"], 1)
                dve.drain()
                dve.tensor_reduce(am[:], xc[:], AX.X, ALU.max, apply_absolute_value=True).then_inc(m["amax"], 1)

            def quantise(g, k):
                dve.wait_ge(m["r1"], g + 1)
                dve.reciprocal(qs[:], mx[:])
                dve.drain()
                dve.scalar_tensor_tensor(qs[:], qs[:], 127.0, rr[:], ALU.mult, ALU.mult)
                dve.drain()
                for j in range(GT):
                    dve.tensor_scalar(xr[:, j, :], xc[:, j, :], qs[:, j:j + 1], ROUND, ALU.mult, ALU.add)
                dve.drain()
                wait(dve, m["qt"], g - 1)
                dve.tensor_scalar(qb[k][:], xr[:], ROUND, None, ALU.subtract).then_inc(m["q"], 1)

            def add_out(g, k):
                dve.wait_ge(m["product"], GT * (g + 1))
                dve.wait_ge(m["xb2"], g + 1)
                for j in range(GT):
                    last = dve.scalar_tensor_tensor(s.xg(g)[:, j, :], OUT[:, P * j:P * j + P], deq2[k][:, j:j + 1], s.xg(g)[:, j, :], ALU.mult, ALU.add)
                last.then_inc(m["x2"], 1)

            def hidden(g, k):
                dve.wait_ge(m["scale"], g + 1)
                for j in range(GT):
                    n = 4 * g + j
                    dve.wait_ge(m["h"], n + 1)
                    wait(dve, m["gelu"], n - 1)
                    dve.scalar_tensor_tensor(hb[j % 2][:], HB[j % 2][:], deq[k][:, j:j + 1], s.bit_b1[:], ALU.mult, ALU.add).then_inc(m["hb"], 1)
                    if j:
                        dve.wait_ge(m["gelu"], n)
                        dve.tensor_reduce(am2[:, j - 1:j], ge[k][:, j - 1, :], AX.X, ALU.max, apply_absolute_value=True).then_inc(m["amax2"], 1)
                dve.wait_ge(m["gelu"], 4 * g + 4)
                dve.tensor_reduce(am2[:, 3:4], ge[k][:, 3, :], AX.X, ALU.max, apply_absolute_value=True).then_inc(m["amax2"], 1)

            def quantise_hidden(g, k):
                dve.wait_ge(m["scale2"], g + 1)
                dve.reciprocal(qs2[:], mx2[:])
                dve.drain()
                dve.scalar_tensor_tensor(qs2[:], qs2[:], 127.0, tmp2[:], ALU.mult, ALU.mult)
                dve.drain()
                for j in range(GT):
                    dve.tensor_scalar(ge[k][:, j, :], ge[k][:, j, :], qs2[:, j:j + 1], ROUND, ALU.mult, ALU.add)
                dve.drain()
                wait(dve, m["q2t"], 4 * (g - 1))
                dve.tensor_scalar(q2[k][:], ge[k][:], ROUND, None, ALU.subtract).then_inc(m["q2"], 1)

            def step(i, k):
                g = 2 * i + k
                more = not (known(i) and g + 1 >= GROUPS)
                if more:
                    prepare(g + 1)
                if not (known(i) and not 0 < g <= GROUPS):
                    quantise_hidden(g - 1, 1 - k)
                if more:
                    quantise(g + 1, 1 - k)
                if not (known(i) and g < 2):
                    add_out(g - 2, k)
                if not (known(i) and g >= GROUPS):
                    hidden(g, k)
            prepare(0)
            quantise(0, 0)
            walk(dve, 0, GROUPS + 2, 2, 2, GROUPS - 2, step)

        @block.scalar
        def _(act):
            def square(g, k, j):
                act.wait_ge(m["gelu"], 4 * g + j + 1)
                act.activation(junk[:, j % 2, :], ge[k][:, j, :], ACT.Square, accum_out=ssq[:, j:j + 1]).then_inc(m["sq"], 1)

            def step(i, k):
                g = 2 * i + k
                if not (known(i) and g >= GROUPS):
                    act.wait_ge(m["qt"], g + 1)
                    wait(act, m["h"], 4 * (g - 1))
                    act.activation(qt[k][:], QT[:, 0:GT * P], ACT.Copy).then_inc(m["qt_copied"], 1)
                    for j in range(GT):
                        act.wait_ge(m["hb"], 4 * g + j + 1)
                        if j == 0:
                            wait(act, m["q2"], g - 1)
                            wait(act, m["scale2"], g)
                        act.activation(ge[k][:, j, :], hb[j % 2][:], ACT.Gelu).then_inc(m["gelu"], 1)
                        if j:
                            square(g, k, j - 1)
                    square(g, k, GT - 1)
                if not (known(i) and g == 0):
                    for j in range(GT):
                        n = 4 * (g - 1) + j
                        act.wait_ge(m["q2t"], n + 1)
                        wait(act, m["product"], n - 1)
                        act.activation(q2t[j % 2][:], T2[j % 2][:, 0:FF].rearrange("p (k c) -> p k c", k=KB), ACT.Copy).then_inc(m["q2t_copied"], 1)
            walk(act, 0, GROUPS + 1, 2, 2, GROUPS - 2, step)

        @block.tensor
        def _(pe):
            def step(i, k):
                g = 2 * i + k
                if not (known(i) and g >= GROUPS):
                    pe.wait_ge(m["q"], g + 1)
                    wait(pe, m["qt_copied"], g)
                    for j in range(GT):
                        last = pe.transpose(QT[:, P * j:P * j + P], qb[k][:, j, :], s.ident_b[:])
                    last.then_inc(m["qt"], 1)
                    pe.wait_ge(m["qt_copied"], g + 1)
                    for j in range(GT):
                        wait(pe, m["hb"], 4 * g + j - 1)
                        pe.matmul(HB[j % 2][:], qt[k][:, P * j:P * j + P], s.bit_w1[:], start=True, stop=True).then_inc(m["h"], 1)
                if not (known(i) and g == 0):
                    pe.wait_ge(m["q2"], g)
                    wait(pe, m["x2"], g - 1)

                    def product(j):
                        pe.wait_ge(m["q2t_copied"], 4 * (g - 1) + j + 1)
                        for b in range(KB):
                            last = pe.matmul(OUT[:, P * j:P * j + P], q2t[j % 2][:, b, :], s.bit_w2[:, b, :], start=b == 0, stop=b == KB - 1)
                        last.then_inc(m["product"], 1)

                    for j in range(GT):
                        n = 4 * (g - 1) + j
                        wait(pe, m["q2t_copied"], n - 1)
                        for b in range(KB):
                            last = pe.transpose(T2[j % 2][:, P * b:P * b + P], q2[1 - k][:, j, P * b:P * b + P], s.ident_b[:])
                        last.then_inc(m["q2t"], 1)
                        if j:
                            product(j - 1)
                    product(GT - 1)
            walk(pe, 0, GROUPS + 1, 2, 2, GROUPS - 2, step)



def cross_attention(nc, s, ctx_in):
    sem = s.sem
    c_loaded = [sem(f"c_ctx_loaded{n}") for n in range(4)]
    names = ("stats rstd kvn kv kvt kvt_copied g g_copied s max exp rden pn pt pt_copied o o_copied w x3")
    m = {n: sem("c_" + n) for n in names.split()}
    CHUNKS = 4 * TILES
    with ExitStack() as ctx:
        sb = lambda name, shape, dt=F32: ctx.enter_context(nc.sbuf_tensor(name, shape, dt))
        cs = [sb(f"c_ctx{n}", [P, D]) for n in range(4)]
        kv = [sb(f"c_kv{n}", [P, 2, D]) for n in range(4)]
        kvt = [sb(f"c_kvT{n}", [P, 4, 64]) for n in range(2)]
        gs = [sb(f"c_g{n}", [P, 2, HEADS1, SEQ]) for n in range(2)]
        pr = [sb(f"c_p{n}", [P, 4, P]) for n in range(4)]
        ptc = [sb(f"c_pT{n}", [P, 4 * P]) for n in range(2)]
        os_ = [sb(f"c_o{n}", [P, HEADS1, P]) for n in range(2)]
        bst = sb("c_bn", [P, 2, 6])
        mv = [sb(f"c_mv{n}", [P, 2, 2]) for n in range(2)]
        rst = [sb(f"c_rstd{n}", [P, 2]) for n in range(2)]
        tmp = sb("c_tmp", [P, 1])
        nmax = [sb(f"c_nmax{n}", [P, 4]) for n in range(4)]
        den = [sb(f"c_den{n}", [P, 4]) for n in range(4)]
        rden = [sb(f"c_rden{n}", [P, 4]) for n in range(4)]
        block = ctx.enter_context(nc.Block())
        GB, SB = s.pb[0:2], s.pb[2:4]
        PT, OB, KVB, WB = s.pb[4:8]
        cvw = ctx_in.rearrange("(t two) s d -> two t s d", two=2)

        def number(i, k, off, limit):
            v = 16 * i + k + off
            return None if known(i) and not 0 <= v < limit else (v, (k + off) % 16)

        def tile(i, k, off):
            if (k + off) % 4:
                return None
            v = 4 * i + (k + off) // 4
            return None if known(i) and not 0 <= v < TILES else (v, (k + off) // 4 % 4, i + (k + off) // 16)

        FIRST, LO, HI, LAST = -9, 16, 240, CHUNKS + 6

        @block.sync
        def _(sp):
            def step(i, k):
                t = 4 * i + k
                if not (known(i) and i == 0):
                    sp.wait_ge(m["kvn"], t - 3)
                sp.dma_start(cs[k][0:64, :], cvw[1, t, :, :]).then_inc(c_loaded[k], 16)
                sp.dma_start(cs[k][64:128, :], cvw[0, t, :, :]).then_inc(c_loaded[k], 16)
            walk(sp, 0, TILES, 4, 4, TILES, step)

        @block.gpsimd
        def _(pool):
            def step(i, k):
                if n := number(i, k, 1, CHUNKS):
                    v, r = n
                    pool.wait_ge(m["rden"], v + 1)
                    pool.tensor_tensor(pr[r % 4][:], pr[r % 4][:], rep(rden[r % 4][:], 2, P), ALU.mult).then_inc(m["pn"], 1)
                if t := tile(i, k, 9):
                    v, r, _ = t
                    a, b = mv[r % 2], rst[r % 2]
                    pool.wait_ge(m["stats"], v + 1)
                    pool.tensor_tensor(b[:], a[:, :, 1], s.eps[:, 0:2], ALU.add)
                    pool.drain()
                    pool.tensor_tensor(b[:], b[:], s.mhalf[:, 0:2], ALU.pow)
                    pool.drain()
                    pool.tensor_tensor(tmp[:], b[:, 0:1], b[:, 0:1], ALU.mult)
                    pool.drain()
                    pool.tensor_tensor(tmp[:], tmp[:], a[:, 0, 1:2], ALU.mult)
                    pool.drain()
                    pool.tensor_scalar(tmp[:], tmp[:], EPS, None, ALU.add)
                    pool.drain()
                    pool.tensor_tensor(tmp[:], tmp[:], s.mhalf[:, 0:1], ALU.pow)
                    pool.drain()
                    pool.tensor_tensor(b[:, 0:1], b[:, 0:1], tmp[:], ALU.mult).then_inc(m["rstd"], 1)
                if t := tile(i, k, 8):
                    v, r, _ = t
                    pool.wait_ge(m["kvn"], v + 1)
                    pool.tensor_tensor(kv[r][:], kv[r][:], s.ln_g[:], ALU.mult)
                    pool.drain()
                    pool.tensor_tensor(kv[r][:], kv[r][:], s.ln_b[:], ALU.add).then_inc(m["kv"], 1)
            walk(pool, FIRST, LAST, 16, LO, HI, step)

        @block.vector
        def _(dve):
            def step(i, k):
                if n := number(i, k, 1, CHUNKS):
                    v, r = n
                    dve.wait_ge(m["exp"], v + 1)
                    dve.reciprocal(rden[r % 4][:], den[r % 4][:]).then_inc(m["rden"], 1)
                if n := number(i, k, 5, CHUNKS):
                    v, r = n
                    dve.wait_ge(m["g"], v + 1)
                    if r % 4 == 0:
                        wait(dve, m["s"], v - 4)
                    q = 4 * (r % 4)
                    dve.tensor_copy(gs[r // 4 % 2][:, :, q:q + 4, :].rearrange("p a h c -> p h a c"),
                                    GB[r % 2][:].rearrange("p (h a c) -> p h a c", h=4, a=2)).then_inc(m["g_copied"], 1)
                if n := number(i, k, 2, CHUNKS):
                    v, r = n
                    dve.wait_ge(m["s"], v + 1)
                    dve.tensor_reduce(nmax[r % 4][:], SB[r % 2][:].rearrange("p (h c) -> p h c", h=4), AX.X, ALU.max, negate=True).then_inc(m["max"], 1)
                if n := number(i, k, -1, CHUNKS):
                    v, r = n
                    dve.wait_ge(m["o"], v + 1)
                    if r % 4 == 0:
                        wait(dve, m["w"], (4 * i + (k - 1) // 4) - 1)
                    half, b = r % 2, r // 2 % 2
                    dve.tensor_copy(os_[r // 4 % 2][:, 8 * half:8 * half + 8, 64 * b:64 * b + 64],
                                    OB[:].rearrange("p (h c) -> p h c", h=8)).then_inc(m["o_copied"], 1)
                if t := tile(i, k, 9):
                    v, r, g = t
                    dve.wait_ge(c_loaded[r], 32 * (g + 1))
                    dve.bn_stats(bst[:, 0, :], s.xg(g)[:, r, :])
                    dve.bn_stats(bst[:, 1, :], cs[r][:])
                    dve.drain()
                    dve.bn_aggr(mv[r % 2][:, 0, :], bst[:, 0, :])
                    dve.bn_aggr(mv[r % 2][:, 1, :], bst[:, 1, :]).then_inc(m["stats"], 1)
                if t := tile(i, k, 8):
                    v, r, g = t
                    a, b = mv[r % 2], rst[r % 2]
                    dve.wait_ge(m["rstd"], v + 1)
                    wait(dve, m["o"], 4 * (v - 3))
                    for half in range(2):
                        rows = slice(64 * half, 64 * half + 64)
                        dve.tensor_scalar(kv[r][rows, half, :], s.xg(g)[rows, r, :], a[rows, 0, 0:1], b[rows, 0:1], ALU.subtract, ALU.mult)
                        last = dve.tensor_scalar(kv[r][rows, 1 - half, :], cs[r][rows, :], a[rows, 1, 0:1], b[rows, 1:2], ALU.subtract, ALU.mult)
                    last.then_inc(m["kvn"], 1)
                if t := tile(i, k, -6):
                    v, r, g = t
                    dve.wait_ge(m["w"], v + 1)
                    dve.tensor_tensor(s.xg(g)[:, r, :], s.xg(g)[:, r, :], WB[:, 0:P], ALU.add).then_inc(m["x3"], 1)
            walk(dve, FIRST, LAST, 16, LO, HI, step)

        @block.scalar
        def _(act):
            def step(i, k):
                if t := tile(i, k, 6):
                    v, r, _ = t
                    act.wait_ge(m["kvt"], v + 1)
                    wait(act, m["s"], 4 * (v - 1))
                    act.activation(kvt[r % 2][:].rearrange("p a c -> p (a c)"), KVB[:, 0:256], ACT.Copy).then_inc(m["kvt_copied"], 1)
                if n := number(i, k, 0, CHUNKS):
                    v, r = n
                    act.wait_ge(m["pt"], v + 1)
                    wait(act, m["o"], v - 1)
                    act.activation(ptc[r % 2][:], PT[:], ACT.Copy).then_inc(m["pt_copied"], 1)
                if n := number(i, k, 2, CHUNKS):
                    v, r = n
                    act.wait_ge(m["max"], v + 1)
                    wait(act, m["pt"], v - 3)
                    for h in range(4):
                        last = act.activation(pr[r % 4][:, h, :], SB[r % 2][:, P * h:P * h + P], ACT.Exp, bias=nmax[r % 4][:, h:h + 1],
                                              accum_out=den[r % 4][:, h:h + 1])
                    last.then_inc(m["exp"], 1)
            walk(act, FIRST, LAST, 16, LO, HI, step)

        @block.tensor
        def _(pe):
            def step(i, k):
                if t := tile(i, k, 6):
                    v, r, _ = t
                    pe.wait_ge(m["kv"], v + 1)
                    wait(pe, m["kvt_copied"], v)
                    for b in range(2):
                        last = pe.transpose(KVB[:, P * b:P * b + P], kv[r][:, b, :], s.ident)
                    last.then_inc(m["kvt"], 1)
                if n := number(i, k, 5, CHUNKS):
                    v, r = n
                    t = r // 4 % 2
                    if r % 4 == 0:
                        pe.wait_ge(m["kvt_copied"], 4 * i + (k + 5) // 4 + 1)
                    wait(pe, m["g_copied"], v - 1)
                    for h in range(4):
                        last = pe.matmul(GB[r % 2][:, P * h:P * h + P].rearrange("p (a c) -> p a c", a=2), s.qk[:, 4 * (r % 4) + h, :], kvt[t][:, 0:4:3, :], start=True, stop=True)
                    last.then_inc(m["g"], 1)
                if n := number(i, k, 2, CHUNKS):
                    v, r = n
                    half, b, t = r % 2, r // 2 % 2, r // 4 % 2
                    pe.wait_ge(m["g_copied"], v + 2 if r % 4 == 0 else v - r % 4 + 4)
                    wait(pe, m["exp"], v - 1)
                    for h in range(4):
                        at = 8 * half + 2 * h
                        last = pe.matmul(SB[r % 2][:, P * h:P * h + P], gs[t][:, b, at:at + 2, :],
                                         kvt[t][:, 2 * b:2 * b + 2, :], start=True, stop=True)
                    last.then_inc(m["s"], 1)
                if n := number(i, k, 0, CHUNKS):
                    v, r = n
                    pe.wait_ge(m["pn"], v + 1)
                    wait(pe, m["pt_copied"], v)
                    for h in range(4):
                        last = pe.transpose(PT[:, P * h:P * h + P], pr[r % 4][:, h, :], s.ident)
                    last.then_inc(m["pt"], 1)
                if t := tile(i, k, -5):
                    v, r, _ = t
                    pe.wait_ge(m["o_copied"], 4 * v + 4)
                    wait(pe, m["x3"], v)
                    for h in range(HEADS1):
                        last = pe.matmul(WB[:, 0:P], os_[r % 2][:, h, :], s.vo[:, h, :], start=h == 0, stop=h == HEADS1 - 1)
                    last.then_inc(m["w"], 1)
                if n := number(i, k, -1, CHUNKS):
                    v, r = n
                    pe.wait_ge(m["pt_copied"], v + 1)
                    wait(pe, m["o_copied"], v)
                    pe.matmul(OB[:], kv[r // 4][:, r // 2 % 2, :], ptc[r % 2][:], start=True, stop=True).then_inc(m["o"], 1)
            walk(pe, FIRST, LAST, 16, LO, HI, step)



def experts(nc, s, out):
    sem = s.sem
    names = ("w_high w_split xt_high xt_split h_high h_split stats rstd xn xt xt_copied logits sorted exp comb combt combt_copied bias b2 h gelu y x4 stored")
    m = {n: sem("d_" + n) for n in names.split()}
    STEPS = EXPERTS * GROUPS
    with ExitStack() as ctx:
        sb = lambda name, shape, dt=F32: ctx.enter_context(nc.sbuf_tensor(name, shape, dt))
        bst = sb("d_bn", [P, GT, 6])
        mv = sb("d_mv", [P, GT, 2])
        rst = sb("d_rstd", [P, GT])
        xn = sb("d_xn", [P, GT, D])
        xt = [sb(f"d_xT{n}", [P, GT * P]) for n in range(2)]
        lg = sb("d_logits", [P, GT, EXPERTS])
        v8 = sb("d_top8", [P, GT, EXPERTS])
        ix = sb("d_idx8", [P, GT, EXPERTS], U32)
        dv = sb("d_dv", [P, GT, EXPERTS])
        ex = sb("d_ex", [P, GT, EXPERTS])
        sm = sb("d_sum", [P, GT])
        gp = sb("d_gates", [P, GT, 2])
        eq = sb("d_eq", [P, 2, GT, EXPERTS])
        comb = [sb(f"d_comb{n}", [P, GT, EXPERTS]) for n in range(2)]
        cbt = sb("d_combT", [EXPERTS, GT * P])
        hf = [sb(f"d_h{n}", [P, KB, GT * P]) for n in range(2)]
        pair = lambda name, shape: [sb(f"{name}_{part}", shape, F16) for part in ("high", "rest")]
        w1 = pair("d_w1", [P, EXPERTS, FF])
        w2 = pair("d_w2", [P, EXPERTS, KB, D])
        xts = [pair(f"d_xTs{n}", [P, GT * P]) for n in range(2)]
        hs = [pair(f"d_hs{n}", [P, KB, GT * P]) for n in range(2)]
        block = ctx.enter_context(nc.Block())
        HB, YB = s.pb[0:4], s.pb[4:6]
        XTB, AUX = s.pb[6:8]
        ov = out.rearrange("(t two) s d -> (two s) t d", two=2)

        def group(i, k, off):
            if (k + off) % 8:
                return None
            v = 2 * i + (k + off) // 8
            return None if known(i) and not 0 <= v < GROUPS else (v, (k + off) // 8 % 2)

        def number(i, k, off):
            v = 16 * i + k + off
            return None if known(i) and not 0 <= v < STEPS else (v, (k + off) % 16)

        FIRST, LO, HI, LAST = -8, 16, 112, STEPS + 2

        @block.sync
        def _(sp):
            with sp.Fori(0, GROUPS) as g:
                sp.wait_ge(m["x4"], EXPERTS * (g + 1))
                sp.dma_start(ov[:, bass.ts(g, GT), :], s.xg(g)).then_inc(m["stored"], 16)
            sp.wait_ge(m["stored"], 16 * GROUPS)

        @block.gpsimd
        def _(pool):
            with pool.Fori(0, GROUPS) as g:
                pool.wait_ge(m["stats"], g + 1)
                pool.tensor_tensor(rst[:], mv[:, :, 1], s.eps[:, 0:GT], ALU.add)
                pool.drain()
                pool.tensor_tensor(rst[:], rst[:], s.mhalf[:, 0:GT], ALU.pow).then_inc(m["rstd"], 1)

        @block.vector
        def _(dve):
            def step(i, k):
                if known(i) and 0 <= 16 * i + k + 6 < EXPERTS:
                    e = 16 * i + k + 6
                    dve.wait_ge(m["w_high"], e + 1)
                    dve.tensor_tensor(w1[1][:, e, :], s.moe_w1[:, e, :], w1[0][:, e, :], ALU.subtract)
                    dve.tensor_tensor(w2[1][:, e, :, :], s.moe_w2[:, e, :, :], w2[0][:, e, :, :], ALU.subtract).then_inc(m["w_split"], 1)
                if t := group(i, k, 5):
                    g, par = t
                    dve.wait_ge(m["xt_high"], g + 1)
                    dve.tensor_tensor(xts[par][1][:], xt[par][:], xts[par][0][:], ALU.subtract).then_inc(m["xt_split"], 1)
                if t := group(i, k, 8):
                    g, _ = t
                    for j in range(GT):
                        dve.bn_stats(bst[:, j, :], s.xg(g)[:, j, :])
                    dve.drain()
                    for j in range(GT):
                        last = dve.bn_aggr(mv[:, j, :], bst[:, j, :])
                    last.then_inc(m["stats"], 1)
                if t := group(i, k, 7):
                    g, _ = t
                    dve.wait_ge(m["rstd"], g + 1)
                    wait(dve, m["xt"], g)
                    for j in range(GT):
                        last = dve.tensor_scalar(xn[:, j, :], s.xg(g)[:, j, :], mv[:, j, 0:1], rst[:, j:j + 1], ALU.subtract, ALU.mult)
                    last.then_inc(m["xn"], 1)
                if t := group(i, k, 4):
                    g, par = t
                    dve.wait_ge(m["logits"], g + 1)
                    dve.tensor_tensor(lg[:], AUX[:, 0:GT * EXPERTS].rearrange("p (j e) -> p j e", j=GT), rep(s.moe_bg[:], 1, GT), ALU.add)
                    dve.drain()
                    for j in range(GT):
                        dve.max(v8[:, j, :], lg[:, j, :])
                    dve.drain()
                    for j in range(GT):
                        dve.max_index(ix[:, j, :], v8[:, j, :], lg[:, j, :])
                    dve.tensor_tensor(dv[:], v8[:], v8[:, :, 0:1].broadcast_to([P, GT, EXPERTS]), ALU.subtract).then_inc(m["sorted"], 1)
                    dve.drain()
                    for c in range(2):
                        dve.tensor_tensor(eq[:, c, :, :], rep(s.iota_8, 1, GT), ix[:, :, c:c + 1].broadcast_to([P, GT, EXPERTS]), ALU.is_equal)
                if t := group(i, k, 3):
                    g, par = t
                    dve.wait_ge(m["exp"], g + 1)
                    dve.tensor_reduce(sm[:], ex[:], AX.X, ALU.add)
                    dve.drain()
                    dve.reciprocal(sm[:], sm[:])
                    dve.drain()
                    dve.tensor_tensor(gp[:], ex[:, :, 0:2], rep(sm[:], 2, 2), ALU.mult)
                    dve.drain()
                    dve.tensor_reduce(sm[:], gp[:], AX.X, ALU.add)
                    dve.drain()
                    dve.tensor_scalar(sm[:], sm[:], 1e-8, None, ALU.add)
                    dve.drain()
                    dve.reciprocal(sm[:], sm[:])
                    dve.drain()
                    dve.tensor_tensor(gp[:], gp[:], rep(sm[:], 2, 2), ALU.mult)
                    dve.drain()
                    for c in range(2):
                        dve.tensor_tensor(eq[:, c, :, :], eq[:, c, :, :], gp[:, :, c:c + 1].broadcast_to([P, GT, EXPERTS]), ALU.mult)
                    dve.drain()
                    dve.tensor_tensor(comb[par][:], eq[:, 0, :, :], eq[:, 1, :, :], ALU.add).then_inc(m["comb"], 1)
                if t := group(i, k, 1):
                    g, _ = t
                    dve.wait_ge(m["bias"], g + 1)
                    dve.tensor_tensor(s.xg(g), s.xg(g), AUX[:].rearrange("p (j d) -> p j d", j=GT), ALU.add).then_inc(m["b2"], 1)
                if n := number(i, k, 0):
                    v, r = n
                    wait(dve, m["y"], v - 1)
                    dve.wait_ge(m["h_high"], v + 1)
                    dve.tensor_tensor(hs[r % 2][1][:, 0:2, :], hf[r % 2][:, 0:2, :], hs[r % 2][0][:, 0:2, :], ALU.subtract)
                    dve.wait_ge(m["gelu"], 4 * v + 4)
                    dve.tensor_copy(hs[r % 2][0][:, 2:4, :], hf[r % 2][:, 2:4, :])
                    dve.drain()
                    dve.tensor_tensor(hs[r % 2][1][:, 2:4, :], hf[r % 2][:, 2:4, :], hs[r % 2][0][:, 2:4, :], ALU.subtract).then_inc(m["h_split"], 1)
                if n := number(i, k, -1):
                    v, r = n
                    g = 2 * i + (k - 1) // 8
                    dve.drain()
                    dve.wait_ge(m["y"], v + 1)
                    for j in range(GT):
                        last = dve.scalar_tensor_tensor(s.xg(g)[:, j, :], YB[r % 2][:, P * j:P * j + P], comb[r // 8][:, j, r % 8:r % 8 + 1],
                                                        s.xg(g)[:, j, :], ALU.mult, ALU.add)
                    last.then_inc(m["x4"], 1)
            walk(dve, FIRST, LAST, 16, LO, HI, step)

        @block.scalar
        def _(act):
            act.wait_ge(s.w_moe, 16 * (2 + 2 * EXPERTS))

            def step(i, k):
                if known(i) and 0 <= 16 * i + k + 8 < EXPERTS:
                    e = 16 * i + k + 8
                    act.activation(w1[0][:, e, :], s.moe_w1[:, e, :], ACT.Copy)
                    act.activation(w2[0][:, e, :, :], s.moe_w2[:, e, :, :], ACT.Copy).then_inc(m["w_high"], 1)
                if n := number(i, k, 0):
                    v, r = n
                    wait(act, m["h_split"], v - 1)
                    for b in range(KB):
                        act.wait_ge(m["h"], 4 * v + b + 1)
                        at = KB * (r % 8) + b
                        act.activation(hf[r % 2][:, b, :], HB[b][:], ACT.Gelu_apprx_tanh, bias=s.moe_b1[:, at:at + 1]).then_inc(m["gelu"], 1)
                        if b == 1:
                            act.drain()
                            wait(act, m["y"], v - 1)
                            act.activation(hs[r % 2][0][:, 0:2, :], hf[r % 2][:, 0:2, :], ACT.Copy).then_inc(m["h_high"], 1)
                if t := group(i, k, 6):
                    g, par = t
                    act.wait_ge(m["xt"], g + 1)
                    wait(act, m["h"], 4 * EXPERTS * (g - 1))
                    act.activation(xt[par][:], XTB[:], ACT.Copy).then_inc(m["xt_copied"], 1)
                    act.drain()
                    act.activation(xts[par][0][:], xt[par][:], ACT.Copy).then_inc(m["xt_high"], 1)
                if t := group(i, k, 4):
                    g, _ = t
                    act.wait_ge(m["sorted"], g + 1)
                    act.activation(ex[:], dv[:], ACT.Exp).then_inc(m["exp"], 1)
                if t := group(i, k, 2):
                    g, _ = t
                    act.wait_ge(m["combt"], g + 1)
                    act.activation(cbt[:], AUX[0:EXPERTS, :], ACT.Copy).then_inc(m["combt_copied"], 1)
            walk(act, FIRST, LAST, 16, LO, HI, step)

        @block.tensor
        def _(pe):
            def step(i, k):
                if n := number(i, k, 0):
                    v, r = n
                    if r % 8 == 0:
                        pe.wait_ge(m["xt_split"], 2 * i + k // 8 + 1)
                    if known(i) and v < EXPERTS:
                        pe.wait_ge(m["w_split"], v + 1)
                    for b in range(KB):
                        wait(pe, m["gelu"], 4 * v + b - 3)
                        parts_product(pe, HB[b][:], [part[:, r % 8, P * b:P * b + P] for part in w1], [part[:] for part in xts[r // 8]]).then_inc(m["h"], 1)
                if t := group(i, k, 6):
                    g, par = t
                    pe.wait_ge(m["xn"], g + 1)
                    wait(pe, m["xt_copied"], g)
                    for j in range(GT):
                        last = pe.transpose(XTB[:, P * j:P * j + P], xn[:, j, :], s.ident)
                    last.then_inc(m["xt"], 1)
                if t := group(i, k, 5):
                    g, par = t
                    if known(g) and g == 0:
                        pe.wait_ge(s.w_moe, 16 * (2 + 2 * EXPERTS))
                    pe.wait_ge(m["xt_copied"], g + 1)
                    wait(pe, m["b2"], g)
                    for j in range(GT):
                        last = pe.matmul(AUX[:, EXPERTS * j:EXPERTS * j + EXPERTS], xt[par][:, P * j:P * j + P], s.moe_wg[:], start=True, stop=True)
                    last.then_inc(m["logits"], 1)
                if t := group(i, k, 2):
                    g, par = t
                    pe.wait_ge(m["comb"], g + 1)
                    for j in range(GT):
                        last = pe.transpose(AUX[0:EXPERTS, P * j:P * j + P], comb[par][:, j, :], s.ident)
                    last.then_inc(m["combt"], 1)
                if t := group(i, k, 1):
                    g, par = t
                    pe.wait_ge(m["combt_copied"], g + 1)
                    for j in range(GT):
                        last = pe.matmul(AUX[:, P * j:P * j + P], cbt[:, P * j:P * j + P], s.moe_b2[:], start=True, stop=True)
                    last.then_inc(m["bias"], 1)
                if n := number(i, k, -1):
                    v, r = n
                    pe.wait_ge(m["h_split"], v + 1)
                    wait(pe, m["x4"], v - 1)
                    for j in range(GT):
                        for b in range(KB):
                            last = parts_product(pe, YB[r % 2][:, P * j:P * j + P], [part[:, b, P * j:P * j + P] for part in hs[r % 2]],
                                                 [part[:, r % 8, b, :] for part in w2], b == 0, b == KB - 1)
                    last.then_inc(m["y"], 1)
            walk(pe, FIRST, LAST, 16, LO, HI, step)



def build(nc, dram, out):
    s = Shared()
    with ExitStack() as ctx:
        def sb(name, shape, dt=F32):
            return ctx.enter_context(nc.sbuf_tensor(name, shape, dt))
        s.sem = lambda name: ctx.enter_context(nc.semaphore(name))
        x = sb("x", [P, GROUPS, GT, D])
        s.xg = lambda g: x[:, g, :, :]
        s.const = sb("const", [P, C_ALL])
        c = s.const
        s.dft_q, s.dft_k, s.dft_inv = c[:, C_DQ:C_DQ + 256], c[:, C_DK:C_DK + 256], c[:, C_INV:C_INV + 64]
        s.ident, s.headmask = c[:, C_ID:C_ID + P], c[:, C_HM:C_HM + P]
        s.iota_e = c[:, C_IE:C_IE + 32].rearrange("p (e i) -> p e i", i=TOP)
        s.row_of = c[:, C_ROW:C_ROW + 64]
        s.iota_8, s.chan = c[:, C_I8:C_I8 + 8], c[:, C_DC:C_DC + 1]
        s.ident_b = sb("ident_bf16", [P, P], BF16)
        s.mhalf = sb("minus_half", [P, 8])
        s.eps = sb("eps", [P, 8])
        s.eps_ff = sb("eps_times_ff", [P, 8])
        s.w_l0 = sb("w_l0", [P, 4, D])
        s.bit_w1 = sb("bit_w1", [P, FF], BF16)
        s.bit_w2 = sb("bit_w2", [P, KB, D], BF16)
        s.bit_b1 = sb("bit_b1", [P, FF])
        s.bit_b2 = sb("bit_b2", [P, D])
        s.bit_ws = sb("bit_w_scale", [P, 2])
        s.ln_g = sb("ln_g", [P, 2, D])
        s.ln_b = sb("ln_b", [P, 2, D])
        s.qk = sb("qk_fused", [P, HEADS1, P])
        s.vo = sb("vo_fused", [P, HEADS1, P])
        s.moe_wg = sb("moe_wg", [P, EXPERTS])
        s.moe_bg = sb("moe_bg", [P, EXPERTS])
        s.moe_w1 = sb("moe_w1", [P, EXPERTS, FF])
        s.moe_b1 = sb("moe_b1", [P, EXPERTS * KB])
        s.moe_w2 = sb("moe_w2", [P, EXPERTS, KB, D])
        s.moe_b2 = sb("moe_b2", [EXPERTS, D])
        s.pb = [ctx.enter_context(nc.psum_tensor(f"bank{n}", [P, 512], F32)) for n in range(8)]
        load_weights(nc, s, dram)
        autocorrelation(nc, s, dram["x"], dram["ctx_1024"])
        bit_ffn(nc, s)
        cross_attention(nc, s, dram["ctx_1024"])
        experts(nc, s, out)


_INS = ["x", "ctx_1024", "L0_xattn_wq", "L0_xattn_wk", "L0_xattn_wv", "L0_xattn_wo", "L0_ffn_w1", "L0_ffn_b1", "L0_ffn_w2",
        "L0_ffn_b2", "L1_xattn_ln1_g", "L1_xattn_ln1_b", "L1_xattn_ln2_g", "L1_xattn_ln2_b", "L1_xattn_Wq", "L1_xattn_Wkv",
        "L1_xattn_Wo", "L1_ffn_Wg", "L1_ffn_bg", "L1_ffn_W1", "L1_ffn_b1", "L1_ffn_W2", "L1_ffn_b2"]


def kernel(**inputs):
    import numpy as _np
    import concourse.bacc as _bacc
    from concourse.bass_utils import run_bass_kernel_spmd as _run

    nc = _bacc.Bacc("TRN2", target_bir_lowering=False, num_devices=1)
    arrays = {"in_" + name: _np.ascontiguousarray(inputs[name]) for name in _INS}
    arrays["in_const"] = constants()
    dram = {name[3:]: nc.dram_tensor(name, a.shape, mybir.dt.from_np(a.dtype), kind="ExternalInput").ap() for name, a in arrays.items()}
    out = nc.dram_tensor("out_x", (BATCH, SEQ, D), F32, kind="ExternalOutput").ap()
    build(nc, dram, out)
    r = _run(nc, [arrays], core_ids=[0])
    return r.results[0]["out_x"]
```
